# Optimizing a Trainium2 kernel written in Bass

```python
import numpy as np
import jax
import jax.numpy as jnp

def _softmax(x, axis=-1):
    return jax.nn.softmax(x, axis=axis)

def _gelu(x):
    return jax.nn.gelu(x, approximate=True)

def _silu(x):
    return jax.nn.silu(x)

def _sigmoid(x):
    return jax.nn.sigmoid(x)

def _layernorm(x, axis=-1, eps=1e-05):
    m = jnp.mean(x, axis=axis, keepdims=True)
    v = jnp.var(x, axis=axis, keepdims=True)
    return (x - m) / jnp.sqrt(v + eps)

def _scatter_add(tgt, idx, src, axis=0):
    return tgt.at[idx].add(src)

def _segment_sum(src, seg, n):
    return jax.ops.segment_sum(src, seg, n)
kernel_name = 'mk_gnn_resnorm_d4_gnn_r32_76b927'

def setup_inputs(seed: int=0):
    np.random.seed(seed)
    _w = jnp.asarray

    def _rec_inputs():
        import jax
        import jax.numpy as jnp
        _gk = jax.random.key(seed)
        x = -0.0003713 + 1 * jax.random.normal(jax.random.fold_in(_gk, 1), (3125, 128), jnp.float32)
        src = jax.random.randint(jax.random.fold_in(_gk, 2), (100000,), 0, 3125, jnp.int32)
        dst = jnp.minimum((3125 * jax.random.uniform(jax.random.fold_in(_gk, 3), (100000,)) ** 2.0).astype(jnp.int32), 99999)
        _o = jnp.argsort(dst, stable=True)
        src = src[_o]
        dst = dst[_o]
        return (x, src, dst)
    x, src, dst = _rec_inputs()

    def _L0_gnn_setup():
        import jax, jax.numpy as jnp
        import numpy as np
        N_NODES = 3125
        N_EDGES = 50000
        IN_CH = 128
        OUT_CH = 128
        BN_EPS = 1e-05
        key = jax.random.key(seed)
        k1, k2, k3 = jax.random.split(key, 3)
        x = jax.random.normal(k1, (N_NODES, IN_CH), dtype=jnp.float32)
        edge_index = jax.random.randint(k2, (2, N_EDGES), 0, N_NODES, dtype=jnp.int64)
        W = jax.random.normal(k3, (OUT_CH, IN_CH), dtype=jnp.float32) * (1.0 / np.sqrt(IN_CH))
        b = jnp.zeros((OUT_CH,), dtype=jnp.float32)
        gamma = jnp.ones((OUT_CH,), dtype=jnp.float32)
        beta = jnp.zeros((OUT_CH,), dtype=jnp.float32)
        return {'x': x, 'edge_index': edge_index, 'W': W, 'b': b, 'gamma': gamma, 'beta': beta}
    _L0_gnn_all = _L0_gnn_setup()
    _L0_gnn_in = {k: v for k, v in _L0_gnn_all.items() if k in ('W', 'b', 'gamma', 'beta')}
    del _L0_gnn_all

    def _L1_gnn_setup():
        import jax, jax.numpy as jnp
        import numpy as np
        N_NODES = 50000
        N_EDGES = 12500
        D_IN = 128

        def _layernorm(x, g, b, eps=1e-05):
            mu = x.mean(-1, keepdims=True)
            var = ((x - mu) ** 2).mean(-1, keepdims=True)
            return (x - mu) * jax.lax.rsqrt(var + eps) * g + b

        def _elu01(x):
            return jnp.where(x > 0, x, 0.1 * jnp.expm1(jnp.minimum(x, 0.0)))

        def _gat_conv(x, src, dst, W, att_src, att_dst, bias, heads, ch, n):
            h = (x @ W).reshape(n, heads, ch)
            a_s = (h * att_src).sum(-1)
            a_d = (h * att_dst).sum(-1)
            e = jax.nn.leaky_relu(a_s[src] + a_d[dst], 0.2)
            m = jax.ops.segment_max(e, dst, num_segments=n)
            ex = jnp.exp(e - m[dst])
            denom = jax.ops.segment_sum(ex, dst, num_segments=n)
            alpha = ex / denom[dst]
            out = jax.ops.segment_sum(alpha[:, :, None] * h[src], dst, num_segments=n)
            return out.reshape(n, heads * ch) + bias
        key = jax.random.key(seed)
        ks = jax.random.split(key, 16)

        def p(k, shape, scale=0.05):
            return scale * jax.random.normal(k, shape, jnp.float32)
        return {'x': jax.random.normal(ks[0], (N_NODES, D_IN), jnp.float32), 'edge_index': jax.random.randint(ks[1], (2, N_EDGES), 0, N_NODES), 'We1': p(ks[2], (128, 128)), 'be1': jnp.zeros(128, jnp.float32), 'ln_g': jnp.ones(128, jnp.float32), 'ln_b': jnp.zeros(128, jnp.float32), 'We2': p(ks[3], (128, 128)), 'be2': jnp.zeros(128, jnp.float32), 'Wg1': p(ks[4], (128, 512)), 'as1': p(ks[5], (2, 256)), 'ad1': p(ks[6], (2, 256)), 'bg1': jnp.zeros(512, jnp.float32), 'Ws1': p(ks[7], (128, 512)), 'bs1': jnp.zeros(512, jnp.float32), 'Wg2': p(ks[8], (512, 256)), 'as2': p(ks[9], (2, 128)), 'ad2': p(ks[10], (2, 128)), 'bg2': jnp.zeros(256, jnp.float32), 'Ws2': p(ks[11], (512, 256)), 'bs2': jnp.zeros(256, jnp.float32), 'Wd1': p(ks[12], (256, 128)), 'bd1': jnp.zeros(128, jnp.float32), 'Wd2': p(ks[13], (128, 128)), 'bd2': jnp.zeros(128, jnp.float32)}
    _L1_gnn_all = _L1_gnn_setup()
    _L1_gnn_in = {k: v for k, v in _L1_gnn_all.items() if k in ('We1', 'be1', 'ln_g', 'ln_b', 'We2', 'be2', 'Wg1', 'as1', 'ad1', 'bg1', 'Ws1', 'bs1', 'Wg2', 'as2', 'ad2', 'bg2', 'Ws2', 'bs2', 'Wd1', 'bd1', 'Wd2', 'bd2')}
    del _L1_gnn_all

    def _L2_gnn_setup():
        import jax, jax.numpy as jnp
        import numpy as np
        N, D, E, OUT = (3125, 128, 18750, 128)
        key = jax.random.key(seed)
        k1, k2, k3, k4, k5 = jax.random.split(key, 5)
        x = jax.random.normal(k1, (N, D), dtype=jnp.float32)
        W = jax.random.normal(k2, (D, OUT), dtype=jnp.float32) * (1.0 / np.sqrt(D))
        b = jax.random.normal(k3, (OUT,), dtype=jnp.float32) * 0.01
        edge_src = jax.random.randint(k4, (E,), 0, N, dtype=jnp.int32)
        edge_dst = jnp.sort(jax.random.randint(k5, (E,), 0, N, dtype=jnp.int32))
        return {'x': x, 'W': W, 'b': b, 'edge_src': edge_src, 'edge_dst': edge_dst}
    _L2_gnn_all = _L2_gnn_setup()
    _L2_gnn_in = {k: v for k, v in _L2_gnn_all.items() if k in ('W', 'b')}
    del _L2_gnn_all

    def _L3_gnn_setup():
        import jax, jax.numpy as jnp
        import numpy as np
        N_NODES = 50000
        N_EDGES = 25000
        IN_DIM = 128
        HID_DIM = 128

        def _gcn_norm(edge_index, num_nodes):
            loop = jnp.arange(num_nodes, dtype=edge_index.dtype)
            row = jnp.concatenate([edge_index[0], loop])
            col = jnp.concatenate([edge_index[1], loop])
            ew = jnp.ones(row.shape[0], jnp.float32)
            deg = jax.ops.segment_sum(ew, col, num_segments=num_nodes)
            dinv = jnp.where(deg > 0, jax.lax.rsqrt(deg), 0.0)
            norm = dinv[row] * ew * dinv[col]
            return (row, col, norm)

        def _gcn_layer(h, W, b, row, col, norm, num_nodes):
            h = h @ W
            msg = h[row] * norm[:, None]
            agg = jax.ops.segment_sum(msg, col, num_segments=num_nodes)
            return agg + b
        key = jax.random.key(seed)
        k0, k1, k2, k3 = jax.random.split(key, 4)
        x = jax.random.normal(k0, (N_NODES, IN_DIM), dtype=jnp.float32)
        edge_index = jax.random.randint(k1, (2, N_EDGES), 0, N_NODES, dtype=jnp.int64)
        lim1 = float(np.sqrt(6.0 / (IN_DIM + HID_DIM)))
        W1 = jax.random.uniform(k2, (IN_DIM, HID_DIM), jnp.float32, -lim1, lim1)
        lim2 = float(np.sqrt(6.0 / (HID_DIM + HID_DIM)))
        W2 = jax.random.uniform(k3, (HID_DIM, HID_DIM), jnp.float32, -lim2, lim2)
        b1 = jnp.zeros((HID_DIM,), jnp.float32)
        b2 = jnp.zeros((HID_DIM,), jnp.float32)
        return {'x': x, 'edge_index': edge_index, 'W1': W1, 'b1': b1, 'W2': W2, 'b2': b2}
    _L3_gnn_all = _L3_gnn_setup()
    _L3_gnn_in = {k: v for k, v in _L3_gnn_all.items() if k in ('W1', 'b1', 'W2', 'b2')}
    del _L3_gnn_all
    return {'x': x, 'src': src, 'dst': dst, 'L0_gnn_W': _L0_gnn_in['W'], 'L0_gnn_b': _L0_gnn_in['b'], 'L0_gnn_gamma': _L0_gnn_in['gamma'], 'L0_gnn_beta': _L0_gnn_in['beta'], 'L1_gnn_We1': _L1_gnn_in['We1'], 'L1_gnn_be1': _L1_gnn_in['be1'], 'L1_gnn_ln_g': _L1_gnn_in['ln_g'], 'L1_gnn_ln_b': _L1_gnn_in['ln_b'], 'L1_gnn_We2': _L1_gnn_in['We2'], 'L1_gnn_be2': _L1_gnn_in['be2'], 'L1_gnn_Wg1': _L1_gnn_in['Wg1'], 'L1_gnn_as1': _L1_gnn_in['as1'], 'L1_gnn_ad1': _L1_gnn_in['ad1'], 'L1_gnn_bg1': _L1_gnn_in['bg1'], 'L1_gnn_Ws1': _L1_gnn_in['Ws1'], 'L1_gnn_bs1': _L1_gnn_in['bs1'], 'L1_gnn_Wg2': _L1_gnn_in['Wg2'], 'L1_gnn_as2': _L1_gnn_in['as2'], 'L1_gnn_ad2': _L1_gnn_in['ad2'], 'L1_gnn_bg2': _L1_gnn_in['bg2'], 'L1_gnn_Ws2': _L1_gnn_in['Ws2'], 'L1_gnn_bs2': _L1_gnn_in['bs2'], 'L1_gnn_Wd1': _L1_gnn_in['Wd1'], 'L1_gnn_bd1': _L1_gnn_in['bd1'], 'L1_gnn_Wd2': _L1_gnn_in['Wd2'], 'L1_gnn_bd2': _L1_gnn_in['bd2'], 'L2_gnn_W': _L2_gnn_in['W'], 'L2_gnn_b': _L2_gnn_in['b'], 'L3_gnn_W1': _L3_gnn_in['W1'], 'L3_gnn_b1': _L3_gnn_in['b1'], 'L3_gnn_W2': _L3_gnn_in['W2'], 'L3_gnn_b2': _L3_gnn_in['b2']}

def reference(x, src, dst, L0_gnn_W, L0_gnn_b, L0_gnn_gamma, L0_gnn_beta, L1_gnn_We1, L1_gnn_be1, L1_gnn_ln_g, L1_gnn_ln_b, L1_gnn_We2, L1_gnn_be2, L1_gnn_Wg1, L1_gnn_as1, L1_gnn_ad1, L1_gnn_bg1, L1_gnn_Ws1, L1_gnn_bs1, L1_gnn_Wg2, L1_gnn_as2, L1_gnn_ad2, L1_gnn_bg2, L1_gnn_Ws2, L1_gnn_bs2, L1_gnn_Wd1, L1_gnn_bd1, L1_gnn_Wd2, L1_gnn_bd2, L2_gnn_W, L2_gnn_b, L3_gnn_W1, L3_gnn_b1, L3_gnn_W2, L3_gnn_b2):
    import jax
    import jax.numpy as jnp

    def _L0_gnn_ref(x, edge_index, W, b, gamma, beta):
        import jax, jax.numpy as jnp
        import numpy as np
        N_NODES = 3125
        N_EDGES = 50000
        IN_CH = 128
        OUT_CH = 128
        BN_EPS = 1e-05
        N = x.shape[0]
        loop = jnp.arange(N, dtype=edge_index.dtype)
        src = jnp.concatenate([edge_index[0], loop])
        dst = jnp.concatenate([edge_index[1], loop])
        deg = jax.ops.segment_sum(jnp.ones_like(dst, dtype=x.dtype), dst, num_segments=N)
        dinv = jnp.where(deg > 0, jax.lax.rsqrt(deg), 0.0)
        norm = dinv[src] * dinv[dst]
        h = x @ W.T
        msg = h[src] * norm[:, None]
        agg = jax.ops.segment_sum(msg, dst, num_segments=N) + b
        r = jax.nn.relu(agg)
        mean = jnp.mean(r, axis=0)
        var = jnp.mean((r - mean) ** 2, axis=0)
        out = (r - mean) * jax.lax.rsqrt(var + BN_EPS) * gamma + beta
        return out

    def _L1_gnn_ref(x, edge_index, We1, be1, ln_g, ln_b, We2, be2, Wg1, as1, ad1, bg1, Ws1, bs1, Wg2, as2, ad2, bg2, Ws2, bs2, Wd1, bd1, Wd2, bd2):
        import jax, jax.numpy as jnp
        import numpy as np
        N_NODES = 50000
        N_EDGES = 12500
        D_IN = 128

        def _layernorm(x, g, b, eps=1e-05):
            mu = x.mean(-1, keepdims=True)
            var = ((x - mu) ** 2).mean(-1, keepdims=True)
            return (x - mu) * jax.lax.rsqrt(var + eps) * g + b

        def _elu01(x):
            return jnp.where(x > 0, x, 0.1 * jnp.expm1(jnp.minimum(x, 0.0)))

        def _gat_conv(x, src, dst, W, att_src, att_dst, bias, heads, ch, n):
            h = (x @ W).reshape(n, heads, ch)
            a_s = (h * att_src).sum(-1)
            a_d = (h * att_dst).sum(-1)
            e = jax.nn.leaky_relu(a_s[src] + a_d[dst], 0.2)
            m = jax.ops.segment_max(e, dst, num_segments=n)
            ex = jnp.exp(e - m[dst])
            denom = jax.ops.segment_sum(ex, dst, num_segments=n)
            alpha = ex / denom[dst]
            out = jax.ops.segment_sum(alpha[:, :, None] * h[src], dst, num_segments=n)
            return out.reshape(n, heads * ch) + bias
        n = x.shape[0]
        h = jax.nn.relu(_layernorm(x @ We1 + be1, ln_g, ln_b)) @ We2 + be2
        loops = jnp.arange(n)
        src = jnp.concatenate([edge_index[0], loops])
        dst = jnp.concatenate([edge_index[1], loops])
        h = _elu01(_gat_conv(h, src, dst, Wg1, as1, ad1, bg1, 2, 256, n) + h @ Ws1 + bs1)
        h = _elu01(_gat_conv(h, src, dst, Wg2, as2, ad2, bg2, 2, 128, n) + h @ Ws2 + bs2)
        return jax.nn.leaky_relu(h @ Wd1 + bd1, 0.1) @ Wd2 + bd2

    def _L2_gnn_ref(x, W, b, edge_src, edge_dst):
        import jax, jax.numpy as jnp
        import numpy as np
        N, D, E, OUT = (3125, 128, 18750, 128)
        n = x.shape[0]
        neigh_sum = jax.ops.segment_sum(x[edge_src], edge_dst, num_segments=n)
        deg = jax.ops.segment_sum(jnp.ones((edge_dst.shape[0],), x.dtype), edge_dst, num_segments=n)
        neigh_mean = neigh_sum / jnp.maximum(deg, 1.0)[:, None]
        h = x + neigh_mean
        return jax.nn.relu(h @ W + b)

    def _L3_gnn_ref(x, edge_index, W1, b1, W2, b2):
        import jax, jax.numpy as jnp
        import numpy as np
        N_NODES = 50000
        N_EDGES = 25000
        IN_DIM = 128
        HID_DIM = 128

        def _gcn_norm(edge_index, num_nodes):
            loop = jnp.arange(num_nodes, dtype=edge_index.dtype)
            row = jnp.concatenate([edge_index[0], loop])
            col = jnp.concatenate([edge_index[1], loop])
            ew = jnp.ones(row.shape[0], jnp.float32)
            deg = jax.ops.segment_sum(ew, col, num_segments=num_nodes)
            dinv = jnp.where(deg > 0, jax.lax.rsqrt(deg), 0.0)
            norm = dinv[row] * ew * dinv[col]
            return (row, col, norm)

        def _gcn_layer(h, W, b, row, col, norm, num_nodes):
            h = h @ W
            msg = h[row] * norm[:, None]
            agg = jax.ops.segment_sum(msg, col, num_segments=num_nodes)
            return agg + b
        n = x.shape[0]
        row, col, norm = _gcn_norm(edge_index, n)
        h = _gcn_layer(x, W1, b1, row, col, norm, n)
        h = jax.nn.relu(h)
        h = _gcn_layer(h, W2, b2, row, col, norm, n)
        return h
    edge_index = jnp.stack([src, dst])
    x = _layernorm(x + _L0_gnn_ref(x, edge_index, L0_gnn_W, L0_gnn_b, L0_gnn_gamma, L0_gnn_beta), axis=-1)
    x = _layernorm(x + _L1_gnn_ref(x, edge_index, L1_gnn_We1, L1_gnn_be1, L1_gnn_ln_g, L1_gnn_ln_b, L1_gnn_We2, L1_gnn_be2, L1_gnn_Wg1, L1_gnn_as1, L1_gnn_ad1, L1_gnn_bg1, L1_gnn_Ws1, L1_gnn_bs1, L1_gnn_Wg2, L1_gnn_as2, L1_gnn_ad2, L1_gnn_bg2, L1_gnn_Ws2, L1_gnn_bs2, L1_gnn_Wd1, L1_gnn_bd1, L1_gnn_Wd2, L1_gnn_bd2), axis=-1)
    x = _layernorm(x + _L2_gnn_ref(x, L2_gnn_W, L2_gnn_b, src, dst), axis=-1)
    x = _layernorm(x + _L3_gnn_ref(x, edge_index, L3_gnn_W1, L3_gnn_b1, L3_gnn_W2, L3_gnn_b2), axis=-1)
    return x

_drawn_inputs = setup_inputs


def setup_inputs(seed=0):
    import zlib

    import numpy as np

    out = dict(_drawn_inputs(seed))
    spreads = {'L0_gnn_b': (0.0, 0.1),
     'L0_gnn_gamma': (1.0, 0.2),
     'L0_gnn_beta': (0.0, 0.1),
     'L1_gnn_be1': (0.0, 0.633),
     'L1_gnn_ln_g': (1.0, 0.6),
     'L1_gnn_ln_b': (0.0, 0.8),
     'L1_gnn_be2': (0.0, 0.39),
     'L1_gnn_bg1': (0.0, 0.297),
     'L1_gnn_bs1': (0.0, 0.1),
     'L1_gnn_bg2': (0.0, 0.308),
     'L1_gnn_bs2': (0.0, 0.1),
     'L1_gnn_bd1': (0.0, 0.1),
     'L1_gnn_bd2': (0.0, 0.1),
     'L3_gnn_b1': (0.0, 0.1),
     'L3_gnn_b2': (0.0, 0.1)}
    factors = {'L1_gnn_as1': 29.171,
     'L1_gnn_ad1': 60.2,
     'L1_gnn_as2': 64.0,
     'L1_gnn_ad2': 64.0,
     'L2_gnn_b': 8.0}
    for name, (base, spread) in spreads.items():
        noise = np.random.default_rng([zlib.crc32(name.encode()), seed]).standard_normal(out[name].shape)
        drawn = base * np.exp(spread * noise) if base else spread * noise
        out[name] = jnp.asarray(drawn.astype(out[name].dtype))
    for name, factor in factors.items():
        out[name] = (out[name] * factor).astype(out[name].dtype)
    return out
```

```python
from contextlib import ExitStack, contextmanager

import concourse.bass as bass
from concourse import mybir

F32 = mybir.dt.float32
BF16 = mybir.dt.bfloat16
F16 = mybir.dt.float16
I32 = mybir.dt.int32
U8 = mybir.dt.uint8
ALU = mybir.AluOpType
ACT = mybir.ActivationFunctionType
AX = mybir.AxisListType.X

P = 128
NODES = 3125
EDGES = 100000
CH = 128
TILES = -(-NODES // P)
PADDED = TILES * P
LAST = NODES - (TILES - 1) * P
BANK = 512
BANKS = -(-NODES // BANK)
LASTBANK = NODES - (BANKS - 1) * BANK
CHUNKS = -(-EDGES // P)
GROUPS = -(-CHUNKS // P)
SHIFT = NODES // 2
STEP = 4
ROUND = float(2 ** 23)
SLOT = TILES * (CH + 1)
EPS = 1e-5


class Kept:
    pass


def bank_width(b):
    return BANK if b < BANKS - 1 else LASTBANK


def make_constants(nc, k):
    step = k.sem("constants_step")
    with nc.Block() as block:
        @block.gpsimd
        def _(pool):
            nc.gpsimd.iota(k.node_number[:, :], [[1, PADDED]], base=-SHIFT, channel_multiplier=0,
                           allow_small_or_imprecise_dtypes=True)
            nc.gpsimd.iota(k.chunk_number[:, :], [[P, GROUPS]], base=0, channel_multiplier=1,
                           allow_small_or_imprecise_dtypes=True)
            nc.gpsimd.iota(k.tile_start[:, :], [[P, TILES]], base=-SHIFT, channel_multiplier=0,
                           allow_small_or_imprecise_dtypes=True)
            nc.gpsimd.memset(k.ones[:, :], 1.0).then_inc(step, 1)
            pool.wait_ge(step, 1)
            nc.gpsimd.affine_select(out=k.ident[:, :], in_=k.ones[:, :], compare_op=ALU.is_equal, fill=0.0,
                                    base=0, pattern=[[-1, P]], channel_multiplier=1).then_inc(step, 1)
            nc.gpsimd.affine_select(out=k.before[:, :], in_=k.ones[0:TILES, 0:TILES + 1], compare_op=ALU.is_gt,
                                    fill=0.0, base=0, pattern=[[1, TILES + 1]], channel_multiplier=-1)
            pool.wait_ge(step, 2)
            nc.gpsimd.tensor_copy(k.ident16[:, :], k.ident[:, :])

        @block.vector
        def _(dve):
            nc.vector.memset(k.dst_rows[:, GROUPS - 1, :], 4 * P * P)
            nc.vector.memset(k.src_rows[:, GROUPS - 1, :], -1)
            nc.vector.memset(k.zeros16[:, :], 0.0)
            nc.vector.memset(k.zeros[:, :], 0.0)
            nc.vector.memset(k.counts_row[:, NODES:PADDED], 0.0)


def load_edges(nc, k):
    loaded = k.sem("edges_loaded")
    whole = (GROUPS - 1) * P * P
    full = EDGES // P - (GROUPS - 1) * P
    tail = EDGES % P
    with nc.Block() as block:
        @block.sync
        def _(sp):
            for rows, edges in ((k.dst_rows, k.dst), (k.src_rows, k.src)):
                sp.dma_start(rows[:, 0:GROUPS - 1, :],
                             edges[0:whole].rearrange("(g p e) -> p g e", p=P, e=P)).then_inc(loaded, 16)
                sp.dma_start(rows[0:full, GROUPS - 1, :],
                             edges[whole:whole + full * P].rearrange("(p e) -> p e", e=P)).then_inc(loaded, 16)
                sp.dma_start(rows[full:full + 1, GROUPS - 1, 0:tail],
                             edges[whole + full * P:EDGES].rearrange("(p e) -> p e", p=1)).then_inc(loaded, 16)
            sp.wait_ge(loaded, 6 * 16)


def make_edge_tables(nc, k):
    step = k.sem("tables_step")
    turned = k.sem("tables_turned")
    dve_done = k.sem("tables_values")
    dst_flat = k.dst_rowsf[:, :, :]
    big = 1.0e6
    with nc.Block() as block:
        @block.vector
        def _(dve):
            nc.vector.tensor_scalar(k.dst_rowsf[:, :, :], k.dst_rows[:, :, :], float(-SHIFT), None,
                                    ALU.add).then_inc(dve_done, 1)
            nc.vector.tensor_scalar(k.src_rowsf[:, :, :], k.src_rows[:, :, :], float(-SHIFT), None,
                                    ALU.add).then_inc(dve_done, 1)
            dve.wait_ge(dve_done, 2)
            nc.vector.tensor_reduce(k.chunk_max[:, :], dst_flat, AX, ALU.max)
            nc.vector.tensor_reduce(k.chunk_min[:, :], dst_flat, AX, ALU.min).then_inc(step, 1)
            nc.vector.tensor_scalar(k.tile_end[:, :], k.tile_start[:, :], float(P), None, ALU.add)
            nc.vector.tensor_scalar(k.chunk_next[:, :], k.chunk_number[:, :], 1.0, None,
                                    ALU.add).then_inc(step, 1)
            dve.wait_ge(step, 2)
            for g in range(GROUPS):
                nc.vector.tensor_scalar(k.cand_lo[:, :, g], k.tile_start[:, :], k.chunk_max[:, g:g + 1], big,
                                        ALU.is_gt, ALU.mult).then_inc(step, 1)
                nc.vector.tensor_scalar(k.cand_hi[:, :, g], k.tile_end[:, :], k.chunk_min[:, g:g + 1],
                                        k.chunk_next[:, g:g + 1], ALU.is_gt, ALU.mult)
            dve.wait_ge(step, 2 + GROUPS)
            for g in range(GROUPS):
                nc.vector.tensor_scalar(k.cand_lo[:, :, g], k.cand_lo[:, :, g], k.chunk_number[:, g:g + 1],
                                        None, ALU.add).then_inc(step, 1)
            dve.wait_ge(step, 2 + 2 * GROUPS)
            nc.vector.tensor_reduce(k.range_part[:, 0, :], k.cand_lo[:, :, :], AX, ALU.min)
            nc.vector.tensor_reduce(k.range_part[:, 1, :], k.cand_hi[:, :, :], AX, ALU.max).then_inc(step, 1)
            base = 3 + 2 * GROUPS
            dve.wait_ge(turned, 2)
            nc.vector.tensor_reduce(k.lo[:, :], k.ps[0:TILES, 4, 0:P], AX, ALU.min).then_inc(step, 1)
            nc.vector.tensor_reduce(k.hi[:, :], k.ps[0:TILES, 5, 0:P], AX, ALU.max).then_inc(step, 1)
            dve.wait_ge(step, base + 2)
            nc.vector.tensor_scalar(k.lo[:, :], k.lo[:, :], float(CHUNKS - 2), None, ALU.min).then_inc(step, 1)
            dve.wait_ge(step, base + 3)
            nc.vector.scalar_tensor_tensor(k.hi[:, :], k.lo[:, :], 1.0, k.hi[:, :], ALU.add,
                                           ALU.max).then_inc(step, 1)
            dve.wait_ge(step, base + 4)
            nc.vector.tensor_tensor(k.take[:, :], k.hi[:, :], k.lo[:, :], ALU.subtract).then_inc(step, 1)
            dve.wait_ge(step, base + 5)
            nc.vector.tensor_scalar(k.take[:, :], k.take[:, :], 1.0 / STEP, (STEP - 1) / (2 * STEP),
                                    ALU.mult, ALU.add).then_inc(step, 1)
            dve.wait_ge(step, base + 6)
            nc.vector.tensor_scalar(k.take[:, :], k.take[:, :], ROUND, None, ALU.add).then_inc(step, 1)
            dve.wait_ge(step, base + 7)
            nc.vector.tensor_scalar(k.take[:, :], k.take[:, :], -ROUND, float(STEP), ALU.add, ALU.mult).then_inc(step, 1)
            dve.wait_ge(turned, 3)
            nc.vector.tensor_copy(k.dst_cols[:, :], k.ps2[:, 0:GROUPS * P])
            nc.vector.tensor_copy(k.src_cols[:, :], k.ps2[:, 2 * BANK:2 * BANK + GROUPS * P])
            dve.wait_ge(turned, 4)
            nc.vector.tensor_copy(k.table[:, 0:TILES + 1], k.ps[0:1, 6, 0:TILES + 1])
            nc.vector.tensor_copy(k.lo_row[:, :], k.ps[0:1, 7, 0:TILES]).then_inc(step, 1)
            dve.wait_ge(step, base + 9)
            nc.vector.tensor_tensor(k.table[:, TILES + 1:2 * TILES + 1], k.lo_row[:, :], k.ps[0:1, 6, 0:TILES],
                                    ALU.subtract)

        @block.tensor
        def _(pe):
            pe.wait_ge(step, 3 + 2 * GROUPS)
            for i in range(2):
                nc.tensor.transpose(k.ps[0:TILES, 4 + i, 0:P], k.range_part[:, i, :],
                                    k.ident[:, :]).then_inc(turned, 1)
            for table, start in ((k.dst_rowsf, 0), (k.src_rowsf, 2 * BANK)):
                for g in range(GROUPS):
                    last = nc.tensor.transpose(k.ps2[:, start + g * P:start + g * P + P], table[:, g, :],
                                               k.ident[:, :])
            last.then_inc(turned, 1)
            pe.wait_ge(step, 3 + 2 * GROUPS + 8)
            nc.tensor.matmul(k.ps[0:1, 6, 0:TILES + 1], k.take[:, :], k.before[:, :], start=True, stop=True)
            nc.tensor.matmul(k.ps[0:1, 7, 0:TILES], k.lo[:, :], k.ident[0:TILES, 0:TILES],
                             start=True, stop=True).then_inc(turned, 1)


SPLIT_BANK = BANKS // 2
PART_BANKS = (range(0, SPLIT_BANK), range(SPLIT_BANK, BANKS))
PART_START = (0, SPLIT_BANK * BANK)
PART_END = (SPLIT_BANK * BANK, NODES)


def build_counts(nc, k):
    onehot_ready = k.sem("onehot_ready")
    onehot_free = k.sem("onehot_free")
    acc_free = k.sem("acc_free")
    rows_ready = k.sem("rows_ready")
    rows_stored = [k.sem(f"rows_stored{i}") for i in range(2)]

    def ranges(eng, j):
        first = eng.value_load(k.table[0:1, bass.ds(j, 1)], min_val=0, max_val=TILES * (GROUPS * P))
        end = eng.value_load(k.table[0:1, bass.ds(j + 1, 1)], min_val=0, max_val=TILES * (GROUPS * P))
        return first, end

    with nc.Block() as block:
        @block.gpsimd
        def _(pool):
            nc.gpsimd.memset(k.scrap[:, 0:1], 0.0).then_inc(onehot_free, STEP)
            nc.gpsimd.memset(k.scrap[:, 1:2], 0.0).then_inc(acc_free, BANKS)
            nc.gpsimd.memset(k.scrap[:, 2:3], 0.0).then_inc(rows_stored[0], 16)
            nc.gpsimd.memset(k.scrap[:, 3:4], 0.0).then_inc(rows_stored[1], 16)

        @block.vector
        def _(dve):
            with dve.Fori(0, TILES) as j:
                first, end = ranges(dve, j)
                shift = dve.value_load(k.table[0:1, bass.ds(j + (TILES + 1), 1)],
                                       min_val=-TILES * GROUPS * P, max_val=GROUPS * P)
                for part, taken in enumerate((first, end)):
                    a, z = PART_START[part], PART_END[part]
                    z += (z - a) % 2
                    with dve.Fori(first, end, STEP) as u:
                        for b in range(STEP):
                            chunk = nc.s_assert_within(
                                u + shift + b, 0, GROUPS * P - 1,
                                skip_runtime_bounds_check_because="ranges end at the last chunk, rounded up to STEP")
                            dve.wait_ge(onehot_free, u + taken + (b + 1))
                            nc.vector.tensor_scalar(k.onehot_dst[:, b, :], k.node_number[:, bass.ds(j * P, P)],
                                                    k.dst_cols[:, bass.ds(chunk, 1)], None, ALU.is_equal)
                            nc.vector.tensor_scalar(k.onehot_src[:, b, 0:z - a], k.node_number[:, a:z],
                                                    k.src_cols[:, bass.ds(chunk, 1)], None,
                                                    ALU.is_equal).then_inc(onehot_ready, 1)

        @block.tensor
        def _(pe):
            with pe.Fori(0, TILES) as j:
                first, end = ranges(pe, j)
                for part, taken in enumerate((first, end)):
                    for b in PART_BANKS[part]:
                        w = bank_width(b)
                        pe.wait_ge(acc_free, j * BANKS + (b + 1))
                        nc.tensor.matmul(k.ps[:, b, 0:w], k.zeros16[:, :], k.node_number[:, 0:w],
                                         start=True, stop=True)
                    with pe.Fori(first, end, STEP) as u:
                        for i in range(STEP):
                            pe.wait_ge(onehot_ready, u + taken + (i + 1))
                            for b in PART_BANKS[part]:
                                w = bank_width(b)
                                at = b * BANK - PART_START[part]
                                last = nc.tensor.matmul(k.ps[:, b, 0:w], k.onehot_dst[:, i, :],
                                                        k.onehot_src[:, i, at:at + w],
                                                        start=False, stop=True, skip_group_check=True)
                            last.then_inc(onehot_free, 1)

        @block.scalar
        def _(act):
            with act.Fori(0, TILES) as j:
                first, end = ranges(act, j)
                for part, taken in enumerate((first, end)):
                    act.wait_ge(onehot_free, end + taken + STEP)
                    act.wait_ge(rows_stored[part], j * 16 + 16)
                    for b in PART_BANKS[part]:
                        w = bank_width(b)
                        nc.scalar.activation(k.counts_row[:, b * BANK:b * BANK + w], k.ps[:, b, 0:w], ACT.Copy,
                                             accum_out=k.deg_part[:, bass.ds(j * BANKS + b, 1)]).then_inc(acc_free, 1)

        @block.sync
        def _(sp):
            with sp.Fori(0, TILES) as j:
                for part in range(2):
                    a, z = PART_START[part], PART_END[part]
                    z = z if part == 0 else PADDED
                    sp.wait_ge(acc_free, j * BANKS + (BANKS + PART_BANKS[part][-1] + 1))
                    sp.dma_start(k.counts_dram[bass.ds(j * P, P), a:z],
                                 k.counts_row[:, a:z]).then_inc(rows_stored[part], 16)
            for part in range(2):
                sp.wait_ge(rows_stored[part], 16 * (TILES + 1))


TURNS = [(q, min(8, TILES - q)) for q in range(0, TILES, 8)]
TURNS_ACT = TURNS[0:2]
TURNS_DVE = TURNS[2:4]


def turn_counts(nc, k):
    row_loaded = [k.sem(f"turn_row{i}_loaded") for i in range(2)]
    act_ready = k.sem("turn_act_ready")
    dve_ready = k.sem("turn_dve_ready")
    act_free = k.sem("turn_act_free")
    dve_free = k.sem("turn_dve_free")

    def banks(parity, n):
        return k.ps[:, 4 * parity + n, :].bitcast(BF16)

    with nc.Block() as block:
        @block.gpsimd
        def _(pool):
            nc.gpsimd.memset(k.scrap[:, 0:1], 0.0).then_inc(act_free, 4)
            nc.gpsimd.memset(k.scrap[:, 1:2], 0.0).then_inc(dve_free, 4)

        def in_pairs(eng, body):
            with eng.Fori(0, TILES - 1, 2) as j:
                body(j, 0)
                body(j + 1, 1)
            body(TILES - 1, 0)

        @block.sync
        def _(sp):
            def load(j, parity):
                sp.wait_ge(dve_free, j * 2 + 2)
                sp.dma_start(k.turn_rows[:, parity, :], k.counts_dram[bass.ds(j * P, P), :]).then_inc(
                    row_loaded[parity], 16)

            in_pairs(sp, load)

        @block.tensor
        def _(pe):
            def turn(j, parity):
                pe.wait_ge(row_loaded[parity], (j - parity) * 8 + 16)
                for n, (q, m) in enumerate(TURNS):
                    if n < 2:
                        pe.wait_ge(act_free, j * 2 + (n + 1))
                    else:
                        pe.wait_ge(dve_free, j * 2 + (n - 1))
                    for i in range(m):
                        last = nc.tensor.transpose(banks(parity, n)[:, i * P:(i + 1) * P],
                                                   k.turn_rows[:, parity, (q + i) * P:(q + i + 1) * P],
                                                   k.ident16[:, :])
                    last.then_inc(act_ready if n < 2 else dve_ready, 1)

            in_pairs(pe, turn)

        def copy_out(eng, copy, turns, first, ready, free):
            def body(j, parity):
                for n, (q, m) in enumerate(turns):
                    eng.wait_ge(ready, j * 2 + (n + 1))
                    copy(k.countsT[:, q:q + m, bass.ds(j * P, P)],
                         banks(parity, first + n)[:, 0:m * P].rearrange("p (t d) -> p t d", d=P)).then_inc(free, 1)
            in_pairs(eng, body)

        @block.scalar
        def _(act):
            copy_out(act, nc.scalar.copy, TURNS_ACT, 0, act_ready, act_free)

        @block.vector
        def _(dve):
            copy_out(dve, nc.vector.tensor_copy, TURNS_DVE, 2, dve_ready, dve_free)


def node_rows(slot, width=CH):
    return slot[:, 0:TILES * width].rearrange("p (t c) -> p t c", c=width)


def over_tiles(row):
    return row[:, :].unsqueeze(1).broadcast_to([P, TILES, row.shape[1]])


def along(col, width=CH):
    return col[:, :].unsqueeze(2).broadcast_to([P, TILES, width])


def load_inputs(nc, k):
    loaded = k.sem("inputs_loaded")
    cleared = k.sem("x_pad_cleared")
    with nc.Block() as block:
        @block.vector
        def _(dve):
            nc.vector.memset(k.x[:, TILES - 1, :], 0.0).then_inc(cleared, 1)

        @block.sync
        def _(sp):
            n = 0
            for tile, source in k.loads:
                sp.dma_start(tile, source, allow_slow_non_contiguous=True).then_inc(loaded, 16)
                n += 1
            sp.dma_start(k.x[:, 0:TILES - 1, :],
                         k.x_dram[0:(TILES - 1) * P, :].rearrange("(t p) c -> p t c", p=P)).then_inc(loaded, 16)
            sp.wait_ge(cleared, 1)
            sp.dma_start(k.x[0:LAST, TILES - 1, :], k.x_dram[(TILES - 1) * P:NODES, :]).then_inc(loaded, 16)
            sp.wait_ge(loaded, 16 * (n + 2))


def turn_rows(nc, k, name, rows, out, padded=True):
    turned = k.sem(f"{name}_turned")
    tiles = [range(4 * b, min(4 * b + 4, TILES)) for b in range(BANKS)]
    with nc.Block() as block:
        @block.tensor
        def _(pe):
            for b in range(BANKS):
                for t in tiles[b]:
                    last = nc.tensor.transpose(k.ps[:, b, (t % 4) * P:(t % 4 + 1) * P], rows[:, t, 0:CH],
                                               k.ident[:, :])
                last.then_inc(turned, 1)

        @block.scalar
        def _(act):
            for b in range(0, BANKS, 2):
                act.wait_ge(turned, b + 1)
                n = len(tiles[b]) * P
                nc.scalar.copy(out[:, b * BANK:b * BANK + n], k.ps[:, b, 0:n])

        @block.vector
        def _(dve):
            for b in range(1, BANKS, 2):
                dve.wait_ge(turned, b + 1)
                n = len(tiles[b]) * P
                nc.vector.tensor_copy(out[:, b * BANK:b * BANK + n], k.ps[:, b, 0:n])


def times_weights(nc, k, name, sources, finish):
    ready = k.sem(f"{name}_ready")
    with nc.Block() as block:
        @block.tensor
        def _(pe):
            for t in range(TILES):
                for i, (rows, weights) in enumerate(sources):
                    last = nc.tensor.matmul(k.ps2[:, t * P:(t + 1) * P], rows[:, t * P:(t + 1) * P], weights,
                                            start=(i == 0), stop=(i == len(sources) - 1))
                if t % 4 == 3 or t == TILES - 1:
                    last.then_inc(ready, 1)

        finish(block, ready)


def layer_norm(nc, k, name, rows, out, gain=None, bias=None):
    step = k.sem(f"{name}_norm_step")
    rooted = k.sem(f"{name}_norm_rooted")
    scaled = k.sem(f"{name}_norm_scaled")
    with nc.Block() as block:
        @block.vector
        def _(dve):
            for t in range(TILES):
                last = nc.vector.bn_stats(k.stats[:, t, :], rows[:, t, 0:CH])
            last.then_inc(step, 1)
            dve.wait_ge(step, 1)
            for t in range(TILES):
                last = nc.vector.bn_aggr(k.moments[:, t, :], k.stats[:, t, :])
            last.then_inc(step, 1)
            dve.wait_ge(step, 2)
            nc.vector.tensor_scalar(k.var[:, :], k.moments[:, :, 1], EPS, None, ALU.add).then_inc(step, 1)
            dve.wait_ge(rooted, 1)
            nc.vector.reciprocal(k.rstd[:, :], k.std[:, :]).then_inc(step, 1)
            dve.wait_ge(step, 4)
            for t in range(TILES):
                last = nc.vector.tensor_scalar(out[:, t, 0:CH], rows[:, t, 0:CH], k.moments[:, t, 0:1],
                                               k.rstd[:, t:t + 1], ALU.subtract, ALU.mult)
            last.then_inc(scaled, 1)
            if gain is not None:
                dve.wait_ge(scaled, 1)
                nc.vector.tensor_tensor(out[:, :, 0:CH], out[:, :, 0:CH], over_tiles(gain), ALU.mult).then_inc(scaled, 1)
                dve.wait_ge(scaled, 2)
                nc.vector.tensor_tensor(out[:, :, 0:CH], out[:, :, 0:CH], over_tiles(bias), ALU.add)

        @block.scalar
        def _(act):
            act.wait_ge(step, 3)
            nc.scalar.activation(k.std[:, :], k.var[:, :], ACT.Sqrt).then_inc(rooted, 1)


def degrees(nc, k):
    step = k.sem("degree_step")
    rooted = k.sem("degree_rooted")
    with nc.Block() as block:
        @block.vector
        def _(dve):
            nc.vector.tensor_reduce(k.deg[:, :], k.deg_part[:, :].rearrange("p (t b) -> p t b", b=BANKS),
                                    AX, ALU.add).then_inc(step, 1)
            dve.wait_ge(step, 1)
            nc.vector.tensor_scalar(k.deg1[:, :], k.deg[:, :], 1.0, None, ALU.add).then_inc(step, 1)
            nc.vector.tensor_scalar(k.degm[:, :], k.deg[:, :], 1.0, None, ALU.max).then_inc(step, 1)
            dve.wait_ge(step, 3)
            nc.vector.reciprocal(k.inv_deg[:, :], k.degm[:, :])
            dve.wait_ge(rooted, 1)
            nc.vector.reciprocal(k.dinv[:, :], k.droot[:, :])

        @block.scalar
        def _(act):
            act.wait_ge(step, 2)
            nc.scalar.activation(k.droot[:, :], k.deg1[:, :], ACT.Sqrt).then_inc(rooted, 1)


def split_rows(nc, k, name, rows, scale, rest):
    step = k.sem(f"{name}_split")
    with nc.Block() as block:
        @block.vector
        def _(dve):
            n = 0
            source = rows
            if scale is not None:
                nc.vector.tensor_tensor(rest[:, :, :], rows[:, :, 0:CH], along(scale), ALU.mult).then_inc(step, 1)
                n += 1
                source = rest
                dve.wait_ge(step, n)
            for i in range(3):
                nc.vector.tensor_copy(k.parts[i][:, :, :], source[:, :, 0:CH]).then_inc(step, 1)
                n += 1
                dve.wait_ge(step, n)
                if i < 2:
                    nc.vector.tensor_tensor(rest[:, :, :], source[:, :, 0:CH], k.parts[i][:, :, :],
                                            ALU.subtract).then_inc(step, 1)
                    n += 1
                    dve.wait_ge(step, n)
                    source = rest


def sum_over_edges(nc, k, name, loops):
    cast = [k.sem(f"{name}_cast{i}") for i in range(2)]
    cast_free = k.sem(f"{name}_cast_free")
    summed = k.sem(f"{name}_summed")
    wide = k.counts_cast

    def in_pairs(eng, body):
        with eng.Fori(0, TILES // 2) as h:
            body(h * 2 + 1, 1)
            body(h * 2 + 2, 0)

    def wait_summed(eng, b):
        if loops:
            eng.wait_ge(summed, b + 1)
        else:
            eng.wait_ge(cast_free, TILES + 2)

    with nc.Block() as block:
        @block.gpsimd
        def _(pool):
            nc.gpsimd.memset(k.aggT[:, NODES:PADDED], 0.0)
            nc.gpsimd.memset(k.scrap[:, 0:1], 0.0).then_inc(cast_free, 2)

        def caster(eng, copy, mine):
            def body(t, parity):
                if parity == mine:
                    eng.wait_ge(cast_free, t + 1)
                    copy(wide[:, parity, 0:NODES + 1],
                         k.countsT[:, bass.ds(t, 1), 0:NODES + 1].rearrange("p t d -> p (t d)")).then_inc(
                             cast[parity], 1)
            if mine == 0:
                body(0, 0)
            in_pairs(eng, body)

        @block.scalar
        def _(act):
            caster(act, nc.scalar.copy, 0)
            for b in range(0, BANKS, 2):
                w = bank_width(b)
                wait_summed(act, b)
                nc.scalar.copy(k.aggT[:, b * BANK:b * BANK + w], k.ps[:, b, 0:w])

        @block.vector
        def _(dve):
            caster(dve, nc.vector.tensor_copy, 1)
            for b in range(1, BANKS, 2):
                w = bank_width(b)
                wait_summed(dve, b)
                nc.vector.tensor_copy(k.aggT[:, b * BANK:b * BANK + w], k.ps[:, b, 0:w])

        @block.tensor
        def _(pe):
            def tile(t, parity, cast_count, first=False):
                pe.wait_ge(cast[parity], cast_count)
                for i in range(3):
                    for b in range(BANKS):
                        w = bank_width(b)
                        last = nc.tensor.matmul(
                            k.ps[:, b, 0:w], k.parts[i][:, bass.ds(t, 1), :].rearrange("p t c -> p (t c)"),
                            wide[:, parity, b * BANK:b * BANK + w], start=(first and i == 0), stop=True,
                            skip_group_check=not (first and i == 0))
                last.then_inc(cast_free, 1)

            tile(0, 0, 1, first=True)
            with pe.Fori(0, TILES // 2) as h:
                tile(h * 2 + 1, 1, h + 1)
                tile(h * 2 + 2, 0, h + 2)
            if loops:
                for t in range(TILES):
                    w = P if t < TILES - 1 else LAST
                    for i in range(3):
                        last = nc.tensor.matmul(k.ps2[:, t * P:t * P + w], k.parts[i][:, t, :],
                                                k.ident16[:, 0:w], start=False, stop=True,
                                                skip_group_check=True)
                    if t % 4 == 3 or t == TILES - 1:
                        last.then_inc(summed, 1)


def to_psum_ready(eng, ready, body):
    for b in range(BANKS):
        eng.wait_ge(ready, b + 1)
        body(range(4 * b, min(4 * b + 4, TILES)))


def gcn_batch_norm_layer(nc, k):
    weights_ready = k.sem("l0_weights_turned")
    split_rows(nc, k, "l0", k.x, k.dinv, k.rows_a)
    sum_over_edges(nc, k, "l0", True)
    with nc.Block() as block:
        @block.tensor
        def _(pe):
            nc.tensor.transpose(k.ps[:, 7, 0:P], k.w_l0[:, :], k.ident[:, :]).then_inc(weights_ready, 1)

        @block.scalar
        def _(act):
            act.wait_ge(weights_ready, 1)
            nc.scalar.copy(k.w_l0t[:, :], k.ps[:, 7, 0:P])
    r = k.rows_a
    r_step = k.sem("l0_relu_step")

    def finish(block, ready):
        @block.vector
        def _(dve):
            def body(tiles):
                for t in tiles:
                    last = nc.vector.scalar_tensor_tensor(r[:, t, :], k.ps2[:, t * P:(t + 1) * P],
                                                          k.dinv[:, t:t + 1], k.b_l0[:, :], ALU.mult, ALU.add)
                last.then_inc(r_step, 1)
            to_psum_ready(dve, ready, body)

        @block.scalar
        def _(act):
            act.wait_ge(r_step, BANKS)
            nc.scalar.activation(r[:, :, :], r[:, :, :], ACT.Relu)

    times_weights(nc, k, "l0", [(k.aggT, k.w_l0t[:, :])], finish)
    total = k.sem("l0_bn_total")
    step = k.sem("l0_bn_step")
    rooted = k.sem("l0_bn_rooted")
    squared = k.rows_b

    def sum_nodes(bank, rows):
        for t in range(TILES):
            n = P if t < TILES - 1 else LAST
            last = nc.tensor.matmul(k.ps[:, bank, 0:CH], k.ones[0:n, :], rows[0:n, t, :], start=(t == 0),
                                    stop=(t == TILES - 1))
        last.then_inc(total, 1)

    with nc.Block() as block:
        @block.tensor
        def _(pe):
            sum_nodes(0, r)
            pe.wait_ge(step, 3)
            sum_nodes(1, squared)

        @block.vector
        def _(dve):
            dve.wait_ge(total, 1)
            nc.vector.tensor_scalar(k.bn_a[:, :], k.ps[:, 0, 0:CH], 1.0 / NODES, None, ALU.mult).then_inc(step, 1)
            dve.wait_ge(step, 1)
            nc.vector.tensor_tensor(r[:, :, :], r[:, :, :], over_tiles(k.bn_a[:, :]), ALU.subtract).then_inc(step, 1)
            dve.wait_ge(step, 2)
            nc.vector.tensor_tensor(squared[:, :, :], r[:, :, :], r[:, :, :], ALU.mult).then_inc(step, 1)
            dve.wait_ge(total, 2)
            nc.vector.tensor_scalar(k.bn_b[:, :], k.ps[:, 1, 0:CH], 1.0 / NODES, EPS, ALU.mult,
                                    ALU.add).then_inc(step, 1)
            dve.wait_ge(rooted, 1)
            nc.vector.reciprocal(k.bn_b[:, :], k.bn_a[:, :]).then_inc(step, 1)
            dve.wait_ge(step, 5)
            nc.vector.tensor_tensor(k.bn_a[:, :], k.bn_b[:, :], k.gamma_l0[:, :], ALU.mult).then_inc(step, 1)
            dve.wait_ge(step, 6)
            nc.vector.tensor_tensor(r[:, :, :], r[:, :, :], over_tiles(k.bn_a[:, :]), ALU.mult).then_inc(step, 1)
            dve.wait_ge(step, 7)
            nc.vector.tensor_tensor(r[:, :, :], r[:, :, :], over_tiles(k.beta_l0[:, :]), ALU.add).then_inc(step, 1)
            dve.wait_ge(step, 8)
            nc.vector.tensor_tensor(r[:, :, :], r[:, :, :], k.x[:, :, :], ALU.add)

        @block.scalar
        def _(act):
            act.wait_ge(step, 4)
            nc.scalar.activation(k.bn_a[:, :], k.bn_b[:, :], ACT.Sqrt).then_inc(rooted, 1)
    layer_norm(nc, k, "l0", r, k.x)


def add_bias_rows(nc, k, name, sources, bias, out, residual=None, relu=False):
    step = k.sem(f"{name}_bias_step")

    def finish(block, ready):
        @block.vector
        def _(dve):
            for b in range(BANKS):
                lo, hi = 4 * b, min(4 * b + 4, TILES)
                dve.wait_ge(ready, b + 1)
                nc.vector.tensor_tensor(out[:, lo:hi, 0:CH],
                                        k.ps2[:, lo * P:hi * P].rearrange("p (t c) -> p t c", c=CH),
                                        bias.unsqueeze(1).broadcast_to([P, hi - lo, CH]), ALU.add).then_inc(step, 1)
            if residual is not None:
                dve.wait_ge(step, BANKS)
                nc.vector.tensor_tensor(out[:, :, 0:CH], out[:, :, 0:CH], residual[:, :, 0:CH], ALU.add)

    times_weights(nc, k, name, sources, finish)


def relu_rows(nc, k, rows):
    with nc.Block() as block:
        @block.scalar
        def _(act):
            nc.scalar.activation(rows[:, :, :], rows[:, :, :], ACT.Relu)


def load_attention(nc, k, slot, source, destination):
    loaded = k.sem(f"attention_loaded_{k.layer}")
    n = source.shape[0] * source.shape[1]
    with nc.Block() as block:
        @block.sync
        def _(sp):
            for i, v in enumerate((source, destination)):
                sp.dma_start(slot[:, i * n:(i + 1) * n],
                             v.rearrange("h c -> (h c)").partition_broadcast(P)).then_inc(loaded, 16)
            sp.wait_ge(loaded, 32)
    scrap = slot[:, 2 * n:2 * n + 2048]
    return (slot[:, 0:n], slot[:, n:2 * n]), scrap


def attention_vectors(nc, k, weights, blocks, vectors, scrap, width):
    with nc.Block() as block:
        @block.vector
        def _(dve):
            for q in range(blocks):
                for i in range(4):
                    head = i % 2
                    nc.vector.tensor_tensor_reduce(scrap[:, (q * 4 + i) * width:(q * 4 + i + 1) * width],
                                                   weights[:, q, head * width:(head + 1) * width],
                                                   vectors[i // 2][:, head * width:(head + 1) * width], 1.0, 0.0,
                                                   ALU.mult, ALU.add, k.att_vec[:, q, i:i + 1])


def scale_sources(nc, k):
    step = k.sem(f"scale_step_{k.layer}")
    turned = k.sem(f"scale_turned_{k.layer}")
    with nc.Block() as block:
        @block.vector
        def _(dve):
            nc.vector.tensor_scalar(k.src_small[:, :, :], k.terms[:, :, 0:2], 0.2, None, ALU.mult)
            by_head = k.terms[:, :, 0:2].rearrange("p t h -> p h t")
            nc.vector.tensor_reduce(k.extremes[:, 0:2], by_head, AX, ALU.max)
            nc.vector.tensor_reduce(k.lowest[:, 0:2], by_head, AX, ALU.min).then_inc(step, 1)
            dve.wait_ge(step, 1)
            nc.vector.tensor_scalar(k.extremes[:, 2:4], k.lowest[:, 0:2], -1.0, None, ALU.mult).then_inc(step, 1)
            dve.wait_ge(turned, 1)
            nc.vector.tensor_reduce(k.extreme_col[:, :], k.ps[0:4, 0, 0:P], AX, ALU.max).then_inc(step, 1)
            dve.wait_ge(step, 3)
            nc.vector.tensor_scalar(k.extreme_diag[:, :], k.ident[0:4, 0:4], k.extreme_col[:, 0:1], None,
                                    ALU.mult).then_inc(step, 1)
            dve.wait_ge(turned, 2)
            nc.vector.tensor_copy(k.extreme[:, :], k.ps[:, 1, 0:4]).then_inc(step, 1)
            dve.wait_ge(step, 5)
            nc.vector.tensor_tensor(k.spread[:, :], k.extreme[:, 0:2], k.extreme[:, 2:4], ALU.add).then_inc(step, 1)
            dve.wait_ge(step, 6)
            nc.vector.tensor_scalar(k.spread[:, :], k.spread[:, :], 2.0, 1e-20, ALU.mult, ALU.max).then_inc(step, 1)
            dve.wait_ge(step, 7)
            nc.vector.reciprocal(k.inv_spread[:, :], k.spread[:, :]).then_inc(step, 1)
            dve.wait_ge(step, 8)
            for h in range(2):
                nc.vector.tensor_scalar(k.src_unit[:, :, h], k.terms[:, :, h], k.extreme[:, 2 + h:3 + h],
                                        k.inv_spread[:, h:h + 1], ALU.add, ALU.mult).then_inc(step, 1)
            dve.wait_ge(step, 10)
            nc.vector.tensor_scalar(k.src_unit[:, :, :], k.src_unit[:, :, :], 0.5, None, ALU.add)

        @block.tensor
        def _(pe):
            pe.wait_ge(step, 2)
            nc.tensor.transpose(k.ps[0:4, 0, 0:P], k.extremes[:, :], k.ident[:, :]).then_inc(turned, 1)
            pe.wait_ge(step, 4)
            nc.tensor.matmul(k.ps[:, 1, 0:4], k.ones[0:4, :], k.extreme_diag[:, :], start=True,
                             stop=True).then_inc(turned, 1)


def attention_maximum(nc, k, head):
    tag = f"{k.layer}{head}"
    scanned = k.sem(f"max_scanned_{tag}")
    turned = k.sem(f"max_turned_{tag}")
    step = k.sem(f"max_step_{tag}")
    best = k.best
    a, b = k.terms[:, :, head], k.terms[:, :, 2 + head]
    with nc.Block() as block:
        @block.vector
        def _(dve):
            nc.vector.memset(best[:, :], 0.0).then_inc(scanned, 1)
            with dve.Fori(0, TILES // 5) as h:
                for i in range(5):
                    t = h * 5
                    dve.wait_ge(scanned, t + (i + 1))
                    nc.vector.scalar_tensor_tensor(best[:, 0:NODES],
                                                   k.countsT[:, bass.ds(t + i, 1), 0:NODES].rearrange("p t d -> p (t d)"),
                                                   k.src_unit[:, bass.ds(t + i, 1), head], best[:, 0:NODES],
                                                   ALU.min, ALU.max).then_inc(scanned, 1)
            dve.wait_ge(turned, 1)
            nc.vector.tensor_reduce(k.node_max[:, :], k.ps2[:, 0:PADDED].rearrange("p (t s) -> p t s", s=P),
                                    AX, ALU.max).then_inc(step, 1)
            dve.wait_ge(step, 1)
            nc.vector.tensor_tensor(k.node_max[:, :], k.node_max[:, :], k.src_unit[:, :, head], ALU.max).then_inc(step, 1)
            dve.wait_ge(step, 2)
            nc.vector.tensor_scalar(k.node_max[:, :], k.node_max[:, :], -0.5, k.spread[:, head:head + 1], ALU.add,
                                    ALU.mult).then_inc(step, 1)
            dve.wait_ge(step, 3)
            nc.vector.tensor_scalar(k.node_max[:, :], k.node_max[:, :], k.extreme[:, 2 + head:3 + head], None,
                                    ALU.subtract).then_inc(step, 1)
            dve.wait_ge(step, 4)
            nc.vector.tensor_tensor(k.node_max[:, :], k.node_max[:, :], b, ALU.add).then_inc(step, 1)
            dve.wait_ge(step, 5)
            nc.vector.scalar_tensor_tensor(k.node_max[:, :], k.node_max[:, :], 0.2, k.node_max[:, :], ALU.mult,
                                           ALU.max).then_inc(step, 1)
            dve.wait_ge(step, 6)
            nc.vector.tensor_tensor(k.dst_one[:, :], b, k.node_max[:, :], ALU.subtract).then_inc(step, 1)
            nc.vector.scalar_tensor_tensor(k.dst_small[:, :], b, 0.2, k.node_max[:, :], ALU.mult,
                                           ALU.subtract).then_inc(step, 1)
            dve.wait_ge(step, 8)
            nc.vector.tensor_tensor(k.own[:, :], a, k.dst_one[:, :], ALU.add).then_inc(step, 1)
            nc.vector.tensor_tensor(k.own_small[:, :], k.src_small[:, :, head], k.dst_small[:, :],
                                    ALU.add).then_inc(step, 1)
            dve.wait_ge(step, 10)
            nc.vector.tensor_tensor(k.own[:, :], k.own[:, :], k.own_small[:, :], ALU.max).then_inc(step, 1)

        @block.tensor
        def _(pe):
            pe.wait_ge(scanned, TILES + 1)
            for t in range(TILES):
                last = nc.tensor.transpose(k.ps2[:, t * P:(t + 1) * P], best[:, t * P:(t + 1) * P], k.ident[:, :])
            last.then_inc(turned, 1)

        @block.scalar
        def _(act):
            act.wait_ge(step, 11)
            nc.scalar.activation(k.own[:, :], k.own[:, :], ACT.Exp)


def spread_node_values(nc, k, name, cols, diagonal, out):
    made = k.sem(f"{name}_diagonal")
    spread = k.sem(f"{name}_spread")
    with nc.Block() as block:
        @block.vector
        def _(dve):
            nc.vector.tensor_tensor(diagonal[:, 0:PADDED].rearrange("p (t d) -> p t d", d=P),
                                    over_tiles(k.ident[:, :]), along(cols), ALU.mult).then_inc(made, 1)
            for b in range(1, BANKS, 2):
                w = bank_width(b)
                dve.wait_ge(spread, b + 1)
                nc.vector.tensor_copy(out[:, b * BANK:b * BANK + w], k.ps[:, b, 0:w])

        @block.tensor
        def _(pe):
            pe.wait_ge(made, 1)
            for b in range(BANKS):
                w = bank_width(b)
                nc.tensor.matmul(k.ps[:, b, 0:w], k.ones[:, :], diagonal[:, b * BANK:b * BANK + w], start=True,
                                 stop=True).then_inc(spread, 1)

        @block.scalar
        def _(act):
            for b in range(0, BANKS, 2):
                w = bank_width(b)
                act.wait_ge(spread, b + 1)
                nc.scalar.copy(out[:, b * BANK:b * BANK + w], k.ps[:, b, 0:w])


HALVES = ((0, TILES // 2 + 1), (TILES // 2 + 1, TILES))
PER_BANK = BANK // (CH + 1)
RING = 3


def attend(nc, k, head, half, features, write_out):
    tag = f"{k.layer}{head}{half}"
    base_ready = k.sem(f"att_base_{tag}")
    arg_ready = k.sem(f"att_arg_{tag}")
    exp_ready = k.sem(f"att_exp_{tag}")
    weight_ready = k.sem(f"att_weight_{tag}")
    weight_free = k.sem(f"att_free_{tag}")
    t0, t1 = HALVES[half]
    d0, d1 = t0 * P, min(t1 * P, NODES)
    n = d1 - d0
    turned = k.sem(f"att_turned_{tag}")
    turned_free = k.sem(f"att_turned_free_{tag}")
    row_ready = k.sem(f"att_row_{tag}")
    step = k.sem(f"att_step_{tag}")

    def in_ring(eng, body):
        with eng.Fori(0, TILES // RING) as h:
            for i in range(RING):
                body(h * RING + i, i)
        for t in range(TILES - TILES % RING, TILES):
            body(t, t % RING)

    def sums(t):
        q = t - t0
        return k.ps[0:P, q // PER_BANK, (q % PER_BANK) * (CH + 1):(q % PER_BANK + 1) * (CH + 1)]

    with nc.Block() as block:
        @block.gpsimd
        def _(pool):
            nc.gpsimd.memset(k.scrap[:, 0:1], 0.0).then_inc(weight_free, RING)
            nc.gpsimd.memset(k.scrap[:, 1:2], 0.0).then_inc(turned_free, 2)

        @block.scalar
        def _(act):
            def body_one(t, i):
                act.wait_ge(weight_free, t + 1)
                nc.scalar.activation(k.ring[:, i, 0:n], k.dst_small_row[:, d0:d1], ACT.Identity,
                                     bias=k.src_small[:, bass.ds(t, 1), head]).then_inc(base_ready, 1)

            def body_exp(t, i):
                act.wait_ge(arg_ready, t + 1)
                nc.scalar.activation(k.ring[:, i, 0:n], k.ring[:, i, 0:n], ACT.Exp).then_inc(exp_ready, 1)

            body_one(0, 0)
            with act.Fori(0, TILES // RING) as h:
                for i in range(RING):
                    t = h * RING
                    body_one(t + (i + 1), (i + 1) % RING)
                    body_exp(t + i, i)
            for t in range(TILES - TILES % RING, TILES):
                if t + 1 < TILES:
                    body_one(t + 1, (t + 1) % RING)
                body_exp(t, t % RING)
            for t in range(t0, t1):
                act.wait_ge(turned, t - t0 + 1)
                write_out(act, t, k.ps[:, 5 + (t - t0) % 2, 0:P]).then_inc(turned_free, 1)

        @block.vector
        def _(dve):
            def arg(t, i):
                dve.wait_ge(base_ready, t + 1)
                nc.vector.scalar_tensor_tensor(k.ring[:, i, 0:n], k.dst_one_row[:, d0:d1],
                                               k.terms[:, bass.ds(t, 1), head], k.ring[:, i, 0:n], ALU.add,
                                               ALU.max).then_inc(arg_ready, 1)

            def weigh(t, i):
                dve.wait_ge(exp_ready, t + 1)
                nc.vector.scalar_tensor_tensor(k.ring[:, i, 0:n], k.ring[:, i, 0:n], 2.0,
                                               k.countsT[:, bass.ds(t, 1), d0:d1].rearrange("p t d -> p (t d)"),
                                               ALU.min, ALU.mult).then_inc(weight_ready, 1)

            arg(0, 0)
            with dve.Fori(0, TILES // RING) as h:
                for i in range(RING):
                    t = h * RING
                    arg(t + (i + 1), (i + 1) % RING)
                    weigh(t + i, i)
            for t in range(TILES - TILES % RING, TILES):
                if t + 1 < TILES:
                    arg(t + 1, (t + 1) % RING)
                weigh(t, t % RING)
            dve.wait_ge(weight_free, TILES + RING)
            for t in range(t0, t1):
                q = t - t0
                nc.vector.scalar_tensor_tensor(k.att_rows[:, q, :], features[:, t, :], k.own[:, t:t + 1],
                                               sums(t), ALU.mult, ALU.add).then_inc(step, 1)
            dve.wait_ge(step, t1 - t0)
            nc.vector.reciprocal(k.att_inv[:, 0:t1 - t0], k.att_rows[:, 0:t1 - t0, CH]).then_inc(step, 1)
            dve.wait_ge(step, t1 - t0 + 1)
            for t in range(t0, t1):
                q = t - t0
                nc.vector.tensor_scalar(k.att_rows[:, q, 0:CH], k.att_rows[:, q, 0:CH], k.att_inv[:, q:q + 1], None,
                                        ALU.mult).then_inc(row_ready, 1)

        @block.tensor
        def _(pe):
            for b in range(-(-(t1 - t0) // PER_BANK)):
                w = min(PER_BANK, t1 - t0 - b * PER_BANK) * (CH + 1)
                nc.tensor.matmul(k.ps[:, b, 0:w], k.zeros[:, :],
                                 features[:, 0:w // (CH + 1), :].rearrange("p t c -> p (t c)"), start=True, stop=True)

            def product(t, i):
                pe.wait_ge(weight_ready, t + 1)
                for q in range(t1 - t0):
                    m = min(P, n - q * P)
                    last = nc.tensor.matmul(sums(t0 + q)[0:m, :], k.ring[:, i, q * P:q * P + m],
                                            features[:, bass.ds(t, 1), :].rearrange("p t c -> p (t c)"),
                                            start=False, stop=True, skip_group_check=True)
                last.then_inc(weight_free, 1)

            in_ring(pe, product)
            for t in range(t0, t1):
                pe.wait_ge(turned_free, t - t0 + 1)
                pe.wait_ge(row_ready, t - t0 + 1)
                nc.tensor.transpose(k.ps[:, 5 + (t - t0) % 2, 0:P], k.att_rows[:, t - t0, 0:CH],
                                    k.ident[:, :]).then_inc(turned, 1)


def elu_banks(nc, k, name, outputs, biases):
    ready = k.sem(f"{name}_ready")
    low_ready = k.sem(f"{name}_low")
    exp_ready = k.sem(f"{name}_exp")
    done = k.sem(f"{name}_done")
    kept = k.sem(f"{name}_kept")
    units = [(o, b) for o in range(len(outputs)) for b in range(BANKS)]
    with nc.Block() as block:
        @block.tensor
        def _(pe):
            for n, (o, b) in enumerate(units):
                w = bank_width(b)
                if n >= 8:
                    pe.wait_ge(kept, n - 7)
                sources = outputs[o][1]
                for i, (weights, rows) in enumerate(sources):
                    last = nc.tensor.matmul(k.ps[:, n % 8, 0:w], weights, rows[:, b * BANK:b * BANK + w],
                                            start=(i == 0), stop=(i == len(sources) - 1))
                last.then_inc(ready, 1)

        @block.vector
        def _(dve):
            def first(n):
                o, b = units[n]
                w = bank_width(b)
                dve.wait_ge(ready, n + 1)
                if n >= 2:
                    dve.wait_ge(done, n - 1)
                nc.vector.tensor_scalar(k.elu_scrap[:, n % 2, 0:w], k.ps[:, n % 8, 0:w], biases[0][:, o:o + 1], 0.0,
                                        ALU.add, ALU.min).then_inc(low_ready, 1)
                nc.vector.tensor_scalar(outputs[o][0][:, b * BANK:b * BANK + w], k.ps[:, n % 8, 0:w],
                                        biases[1][:, o:o + 1], -0.1, ALU.add, ALU.max).then_inc(kept, 1)

            def second(n):
                o, b = units[n]
                w = bank_width(b)
                out = outputs[o][0][:, b * BANK:b * BANK + w]
                dve.wait_ge(exp_ready, n + 1)
                dve.wait_ge(kept, n + 1)
                nc.vector.scalar_tensor_tensor(out, k.elu_scrap[:, n % 2, 0:w], 0.1, out, ALU.mult,
                                               ALU.add).then_inc(done, 1)

            for n in range(len(units) + 1):
                if n < len(units):
                    first(n)
                if n >= 1:
                    second(n - 1)

        @block.scalar
        def _(act):
            for n, (o, b) in enumerate(units):
                w = bank_width(b)
                act.wait_ge(low_ready, n + 1)
                nc.scalar.activation(k.elu_scrap[:, n % 2, 0:w], k.elu_scrap[:, n % 2, 0:w],
                                     ACT.Exp).then_inc(exp_ready, 1)


def first_attention(nc, k):
    S = k.slots
    h_rows, h_chan = node_rows(S[2], CH + 1), S[1]
    turn_rows(nc, k, "e_x", k.x, S[1])
    z = k.rows_a
    add_bias_rows(nc, k, "e_in", [(S[1], k.w_e1[:, :])], k.b_e1[:, :], z)
    layer_norm(nc, k, "e_in", z, z, k.ln_g[:, :], k.ln_b[:, :])
    relu_rows(nc, k, z)
    turn_rows(nc, k, "e_z", z, S[4])
    add_bias_rows(nc, k, "e_h", [(S[4], k.w_e2[:, :])], k.b_e2[:, :], h_rows)
    with nc.Block() as block:
        @block.gpsimd
        def _(pool):
            nc.gpsimd.memset(h_rows[:, :, CH], 1.0)
    turn_rows(nc, k, "e_h", h_rows, h_chan)

    k.layer = "a"
    vectors, scrap = load_attention(nc, k, S[5], k.as1, k.ad1)
    attention_vectors(nc, k, k.w_g1[:, :].unsqueeze(1), 1, vectors, scrap, 256)
    terms_ready = k.sem("terms_ready_a")
    with nc.Block() as block:
        @block.tensor
        def _(pe):
            for t in range(TILES):
                last = nc.tensor.matmul(k.ps[:, 0, t * 4:t * 4 + 4], h_chan[:, t * P:(t + 1) * P],
                                        k.att_vec[:, 0, :], start=True, stop=True)
            last.then_inc(terms_ready, 1)

        @block.vector
        def _(dve):
            dve.wait_ge(terms_ready, 1)
            nc.vector.tensor_copy(k.terms[:, :, :], k.ps[:, 0, 0:TILES * 4].rearrange("p (t i) -> p t i", i=4))
            nc.vector.tensor_tensor(k.bias_a[:, :], k.b_g1[:, :], k.b_s1[:, :], ALU.add)
            nc.vector.tensor_tensor(k.bias_b[:, :], k.b_g2[:, :], k.b_s2[:, :], ALU.add)
    with nc.Block() as block:
        @block.vector
        def _(dve):
            nc.vector.tensor_scalar(k.bias_a_low[:, :], k.bias_a[:, :], -0.1, None, ALU.add)
    scale_sources(nc, k)
    k.dst_one_row, k.dst_small_row = S[3], S[4]
    gathered = (S[7], S[3])
    k.best = S[4]
    for head in range(2):
        attention_maximum(nc, k, head)
        spread_node_values(nc, k, f"one_a{head}", k.dst_one[:, :], S[5], k.dst_one_row)
        spread_node_values(nc, k, f"small_a{head}", k.dst_small[:, :], S[5], k.dst_small_row)
        for half in range(2):
            def write_out(act, t, turned, head=head):
                w = min(P, NODES - t * P)
                return nc.scalar.copy(gathered[head][:, t * P:t * P + w], turned[:, 0:w])
            attend(nc, k, head, half, h_rows, write_out)
    return h_chan, gathered


def second_attention(nc, k, h_chan, gathered):
    S = k.slots
    h2 = (S[2], S[4], S[5], S[6])
    with nc.Block() as block:
        @block.gpsimd
        def _(pool):
            for rows in h2:
                nc.gpsimd.memset(rows[:, NODES:PADDED], 0.0)
    elu_banks(nc, k, "e_elu1", [
        (h2[o], [(k.w_g1[:, o * P:(o + 1) * P], gathered[o // 2]), (k.w_s1[:, o * P:(o + 1) * P], h_chan)])
        for o in range(4)], (k.bias_a, k.bias_a_low))

    k.layer = "b"
    parked = k.sem("x_parked")
    with nc.Block() as block:
        @block.sync
        def _(sp):
            sp.dma_start(k.x_park, k.x[:, :, :]).then_inc(parked, 16)
            sp.wait_ge(parked, 16)
    vectors, scrap = load_attention(nc, k, S[7], k.as2, k.ad2)
    attention_vectors(nc, k, k.w_g2, 4, vectors, scrap, 128)
    features = (node_rows(S[1], CH + 1), node_rows(S[3], CH + 1))
    skips = (S[7], S[0])
    ready = k.sem("g2_ready")
    act_copied = k.sem("g2_act_copied")
    dve_copied = k.sem("g2_dve_copied")
    ready_terms = k.sem("g2_terms_ready")
    with nc.Block() as block:
        @block.tensor
        def _(pe):
            for t in range(TILES):
                b = t % 6
                if t >= 6:
                    pe.wait_ge(dve_copied if t % 2 else act_copied, (t - 6) // 2 + 1)
                for q in range(4):
                    last = nc.tensor.matmul(k.ps[:, b, 0:256], h2[q][:, t * P:(t + 1) * P], k.w_g2[:, q, :],
                                            start=(q == 0), stop=(q == 3))
                last.then_inc(ready, 1)
            for t in range(TILES):
                for q in range(4):
                    last = nc.tensor.matmul(k.ps[:, 7, t * 4:t * 4 + 4], h2[q][:, t * P:(t + 1) * P],
                                            k.att_vec[:, q, :], start=(q == 0), stop=(q == 3))
            last.then_inc(ready_terms, 1)

        @block.scalar
        def _(act):
            for t in range(0, TILES, 2):
                act.wait_ge(ready, t + 1)
                nc.scalar.copy(features[0][:, t, 0:CH], k.ps[:, t % 6, 0:CH])
                nc.scalar.copy(features[1][:, t, 0:CH], k.ps[:, t % 6, CH:2 * CH]).then_inc(act_copied, 1)

        @block.vector
        def _(dve):
            for t in range(1, TILES, 2):
                dve.wait_ge(ready, t + 1)
                nc.vector.tensor_copy(features[0][:, t, 0:CH], k.ps[:, t % 6, 0:CH])
                nc.vector.tensor_copy(features[1][:, t, 0:CH], k.ps[:, t % 6, CH:2 * CH]).then_inc(dve_copied, 1)
            dve.wait_ge(ready_terms, 1)
            nc.vector.tensor_copy(k.terms[:, :, :], k.ps[:, 7, 0:TILES * 4].rearrange("p (t i) -> p t i", i=4))

        @block.gpsimd
        def _(pool):
            for f in features:
                nc.gpsimd.memset(f[:, :, CH], 1.0)
    ready2 = k.sem("skip_ready")
    for o in range(2):
        with nc.Block() as block:
            @block.tensor
            def _(pe, o=o):
                for b in range(BANKS):
                    w = bank_width(b)
                    for q in range(4):
                        last = nc.tensor.matmul(k.ps[:, b, 0:w], k.w_s2[:, q, o * P:(o + 1) * P],
                                                h2[q][:, b * BANK:b * BANK + w], start=(q == 0), stop=(q == 3))
                    last.then_inc(ready2, 1)

            @block.scalar
            def _(act, o=o):
                for b in range(BANKS):
                    w = bank_width(b)
                    act.wait_ge(ready2, BANKS * o + b + 1)
                    nc.scalar.activation(skips[o][:, b * BANK:b * BANK + w], k.ps[:, b, 0:w], ACT.Identity,
                                         bias=k.bias_b[:, o:o + 1])
    scale_sources(nc, k)
    k.dst_one_row, k.dst_small_row, k.best = S[2], S[4], S[4]
    k.turned_tile = S[2]
    for head in range(2):
        attention_maximum(nc, k, head)
        spread_node_values(nc, k, f"one_b{head}", k.dst_one[:, :], S[5], k.dst_one_row)
        spread_node_values(nc, k, f"small_b{head}", k.dst_small[:, :], S[5], k.dst_small_row)
        for half in range(2):
            def write_out(act, t, turned):
                w = min(P, NODES - t * P)
                return nc.scalar.copy(k.dst_one_row[:, t * P:t * P + w], turned[:, 0:w])
            attend(nc, k, head, half, features[head], write_out)
        step = k.sem(f"elu_b{head}_step")
        exped = k.sem(f"elu_b{head}_exp")
        y, g, low = skips[head], k.dst_one_row, S[5]
        with nc.Block() as block:
            @block.vector
            def _(dve, y=y, g=g, low=low, step=step, exped=exped):
                nc.vector.memset(y[:, NODES:PADDED], 0.0)
                nc.vector.tensor_tensor(y[:, 0:NODES], y[:, 0:NODES], g[:, 0:NODES], ALU.add).then_inc(step, 1)
                dve.wait_ge(step, 1)
                nc.vector.tensor_scalar(low[:, 0:NODES], y[:, 0:NODES], 0.0, None, ALU.min).then_inc(step, 1)
                dve.wait_ge(step, 2)
                nc.vector.tensor_scalar(y[:, 0:NODES], y[:, 0:NODES], 0.0, -0.1, ALU.max, ALU.add).then_inc(step, 1)
                dve.wait_ge(exped, 1)
                dve.wait_ge(step, 3)
                nc.vector.scalar_tensor_tensor(y[:, 0:NODES], low[:, 0:NODES], 0.1, y[:, 0:NODES], ALU.mult, ALU.add)

            @block.scalar
            def _(act, low=low, step=step, exped=exped):
                act.wait_ge(step, 2)
                nc.scalar.activation(low[:, 0:NODES], low[:, 0:NODES], ACT.Exp).then_inc(exped, 1)

    d_ready = k.sem("dec_ready")
    d_step = k.sem("dec_step")
    y1 = S[2]
    with nc.Block() as block:
        @block.tensor
        def _(pe):
            for b in range(BANKS):
                w = bank_width(b)
                for q in range(2):
                    last = nc.tensor.matmul(k.ps[:, b, 0:w], k.w_d1[:, q, :], skips[q][:, b * BANK:b * BANK + w],
                                            start=(q == 0), stop=(q == 1))
                last.then_inc(d_ready, 1)

        @block.vector
        def _(dve):
            nc.vector.memset(y1[:, NODES:PADDED], 0.0)
            for b in range(BANKS):
                w = bank_width(b)
                dve.wait_ge(d_ready, b + 1)
                nc.vector.tensor_scalar(y1[:, b * BANK:b * BANK + w], k.ps[:, b, 0:w], k.b_d1[:, 0:1], None,
                                        ALU.add).then_inc(d_step, 1)
            dve.wait_ge(d_step, BANKS)
            nc.vector.scalar_tensor_tensor(y1[:, 0:NODES], y1[:, 0:NODES], 0.1, y1[:, 0:NODES], ALU.mult, ALU.max)
    fetched = k.sem("x_fetched")
    with nc.Block() as block:
        @block.sync
        def _(sp):
            sp.dma_start(k.x[:, :, :], k.x_park).then_inc(fetched, 16)
            sp.wait_ge(fetched, 16)
    add_bias_rows(nc, k, "e_out", [(y1, k.w_d2[:, :])], k.b_d2[:, :], k.rows_a, residual=k.x)
    layer_norm(nc, k, "e_out", k.rows_a, k.x)


def load_late_weights(nc, k):
    loaded = k.sem("late_loaded")
    with nc.Block() as block:
        @block.sync
        def _(sp):
            for tile, source in k.late_loads:
                sp.dma_start(tile, source).then_inc(loaded, 16)
            sp.wait_ge(loaded, 16 * len(k.late_loads))


def mean_layer(nc, k):
    split_rows(nc, k, "l2", k.x, None, k.rows_a)
    sum_over_edges(nc, k, "l2", False)
    turn_rows(nc, k, "l2_x", k.x, k.slots[6])
    step = k.sem("l2_step")
    add_bias_rows(nc, k, "l2_own", [(k.slots[6], k.w_l2[:, :])], k.b_l2[:, :], k.rows_a)

    def finish(block, ready):
        @block.vector
        def _(dve):
            def body(tiles):
                for t in tiles:
                    last = nc.vector.scalar_tensor_tensor(k.rows_a[:, t, :], k.ps2[:, t * P:(t + 1) * P],
                                                          k.inv_deg[:, t:t + 1], k.rows_a[:, t, :], ALU.mult,
                                                          ALU.add)
                last.then_inc(step, 1)
            to_psum_ready(dve, ready, body)
            dve.wait_ge(step, BANKS)
            nc.vector.scalar_tensor_tensor(k.rows_a[:, :, :], k.rows_a[:, :, :], 0.0, k.x[:, :, :], ALU.max, ALU.add)

    times_weights(nc, k, "l2_mean", [(k.aggT, k.w_l2[:, :])], finish)
    layer_norm(nc, k, "l2", k.rows_a, k.x)


def gcn_layer(nc, k):
    split_rows(nc, k, "l3a", k.x, k.dinv, k.rows_a)
    sum_over_edges(nc, k, "l3a", True)
    step = k.sem("l3_step")

    def finish_first(block, ready):
        @block.vector
        def _(dve):
            def body(tiles):
                for t in tiles:
                    last = nc.vector.scalar_tensor_tensor(k.rows_b[:, t, :], k.ps2[:, t * P:(t + 1) * P],
                                                          k.dinv[:, t:t + 1], k.b_l3a[:, :], ALU.mult, ALU.add)
                last.then_inc(step, 1)
            to_psum_ready(dve, ready, body)

        @block.scalar
        def _(act):
            act.wait_ge(step, BANKS)
            nc.scalar.activation(k.rows_b[:, :, :], k.rows_b[:, :, :], ACT.Relu)

    times_weights(nc, k, "l3a", [(k.aggT, k.w_l3a[:, :])], finish_first)
    split_rows(nc, k, "l3b", k.rows_b, k.dinv, k.rows_a)
    sum_over_edges(nc, k, "l3b", True)

    def finish_second(block, ready):
        @block.vector
        def _(dve):
            def body(tiles):
                for t in tiles:
                    last = nc.vector.scalar_tensor_tensor(k.rows_b[:, t, :], k.ps2[:, t * P:(t + 1) * P],
                                                          k.dinv[:, t:t + 1], k.b_l3b[:, :], ALU.mult, ALU.add)
                last.then_inc(step, 1)
            for b in range(BANKS):
                dve.wait_ge(ready, b + 1)
                body(range(4 * b, min(4 * b + 4, TILES)))
            dve.wait_ge(step, 2 * BANKS)
            nc.vector.tensor_tensor(k.rows_b[:, :, :], k.rows_b[:, :, :], k.x[:, :, :], ALU.add)

    times_weights(nc, k, "l3b", [(k.aggT, k.w_l3b[:, :])], finish_second)
    layer_norm(nc, k, "l3", k.rows_b, k.x)


def store_output(nc, k):
    stored = k.sem("output_stored")
    with nc.Block() as block:
        @block.sync
        def _(sp):
            sp.dma_start(k.out[0:(TILES - 1) * P, :].rearrange("(t p) c -> p t c", p=P),
                         k.x[:, 0:TILES - 1, :]).then_inc(stored, 16)
            sp.dma_start(k.out[(TILES - 1) * P:NODES, :], k.x[0:LAST, TILES - 1, :]).then_inc(stored, 16)
            sp.wait_ge(stored, 32)


def place(nc, ctx, k):
    def sb(name, shape, dt=F32):
        return ctx.enter_context(nc.sbuf_tensor(name, shape, dt))

    k.countsT = sb("countsT", [P, TILES, PADDED], U8)
    arena = sb("arena", [P, 8 * SLOT])
    k.slots = [arena[:, i * SLOT:(i + 1) * SLOT] for i in range(8)]
    k.psum = ctx.enter_context(nc.psum_tensor("ps", [P, 8, BANK], F32))
    k.ps = k.psum
    k.ps2 = k.psum[:, :, :].rearrange("p b c -> p (b c)")
    k.counts_dram = nc.dram_tensor("counts_rows", (PADDED, PADDED), BF16, kind="Internal").ap()
    k.x_park = nc.dram_tensor("x_park", (P, TILES, CH), F32, kind="Internal").ap()

    k.ident, k.ones, k.zeros = sb("ident", [P, P]), sb("ones", [P, P]), sb("zeros", [P, P])
    k.ident16 = sb("ident16", [P, P], BF16)
    k.scrap = sb("scrap", [P, 4])
    k.deg, k.deg1, k.degm = (sb("deg", [P, TILES]), sb("deg1", [P, TILES]), sb("degm", [P, TILES]))
    k.droot, k.inv_deg, k.dinv = (sb("droot", [P, TILES]), sb("inv_deg", [P, TILES]), sb("dinv", [P, TILES]))
    k.var, k.std, k.rstd = (sb("var", [P, TILES]), sb("std", [P, TILES]), sb("rstd", [P, TILES]))
    k.node_max, k.dst_one, k.dst_small = (sb("node_max", [P, TILES]), sb("dst_one", [P, TILES]), sb("dst_small", [P, TILES]))
    k.own, k.own_small, k.att_inv = (sb("own", [P, TILES]), sb("own_small", [P, TILES]), sb("att_inv", [P, TILES]))
    k.deg_part = sb("deg_part", [P, TILES * BANKS])
    k.stats, k.moments = sb("stats", [P, TILES, 6]), sb("moments", [P, TILES, 2])
    k.terms = sb("terms", [P, TILES, 4])
    k.src_small, k.src_unit = sb("src_small", [P, TILES, 2]), sb("src_unit", [P, TILES, 2])
    k.extremes, k.extreme, k.lowest = sb("extremes", [P, 4]), sb("extreme", [P, 4]), sb("lowest", [P, 2])
    k.extreme_col, k.extreme_diag = sb("extreme_col", [4, 1]), sb("extreme_diag", [4, 4])
    k.spread, k.inv_spread = sb("spread", [P, 2]), sb("inv_spread", [P, 2])
    k.att_vec = sb("att_vec", [P, 4, 4])
    k.bias_a, k.bias_a_low, k.bias_b = sb("bias_a", [P, 4]), sb("bias_a_low", [P, 4]), sb("bias_b", [P, 2])
    k.elu_scrap = sb("elu_scrap", [P, 2, BANK])

    i = k.inputs
    k.w_e1, k.w_e2, k.w_d2 = sb("w_e1", [P, CH]), sb("w_e2", [P, CH]), sb("w_d2", [P, CH])
    k.w_g1, k.w_s1 = sb("w_g1", [P, 512]), sb("w_s1", [P, 512])
    k.w_g2, k.w_s2, k.w_d1 = sb("w_g2", [P, 4, 256]), sb("w_s2", [P, 4, 256]), sb("w_d1", [P, 2, CH])
    k.b_e1, k.b_e2, k.b_d2 = sb("b_e1", [P, CH]), sb("b_e2", [P, CH]), sb("b_d2", [P, CH])
    k.ln_g, k.ln_b = sb("ln_g", [P, CH]), sb("ln_b", [P, CH])
    k.b_g1, k.b_s1, k.b_g2, k.b_s2 = sb("b_g1", [P, 4]), sb("b_s1", [P, 4]), sb("b_g2", [P, 2]), sb("b_s2", [P, 2])
    k.b_d1 = sb("b_d1", [P, 1])
    k.as1, k.ad1, k.as2, k.ad2 = i["L1_gnn_as1"], i["L1_gnn_ad1"], i["L1_gnn_as2"], i["L1_gnn_ad2"]

    S = k.slots
    k.x = node_rows(S[0])
    half = SLOT // 2
    k.parts = [S[1][:, 0:half - half % 4].bitcast(BF16), S[1][:, half + 1:2 * half + 1].bitcast(BF16),
               S[2][:, 0:half - half % 4].bitcast(BF16)]
    k.parts = [p[:, 0:PADDED].rearrange("p (t c) -> p t c", c=CH) for p in k.parts]
    k.rows_a, k.rows_b = node_rows(S[3]), node_rows(S[7])
    k.counts_cast = S[4][:, 0:PADDED].bitcast(BF16).rearrange("p (b d) -> p b d", b=2)
    k.aggT = S[5]
    late = [S[2][:, half + 1 + n * CH:half + 1 + (n + 1) * CH] for n in range(6)]
    k.w_l2, k.w_l3a, k.w_l3b, k.b_l2, k.b_l3a, k.b_l3b = late
    first = [S[6][:, n * CH:(n + 1) * CH] for n in range(7)]
    k.w_l0, k.w_l0t, k.b_l0, k.gamma_l0, k.beta_l0, k.bn_a, k.bn_b = first
    k.ring = arena[:, 5 * SLOT:5 * SLOT + RING * 13 * P].rearrange("p (r d) -> p r d", r=RING)
    k.att_rows = arena[:, 5 * SLOT:5 * SLOT + 13 * (CH + 1)].rearrange("p (t c) -> p t c", c=CH + 1)

    def row(name):
        return i[name].partition_broadcast(P)

    def cols(name):
        return i[name].rearrange("(o p) -> p o", p=P)

    k.loads = [
        (k.w_l0, i["L0_gnn_W"]), (k.b_l0, row("L0_gnn_b")), (k.gamma_l0, row("L0_gnn_gamma")),
        (k.beta_l0, row("L0_gnn_beta")),
        (k.w_e1[:, :], i["L1_gnn_We1"]), (k.b_e1[:, :], row("L1_gnn_be1")), (k.ln_g[:, :], row("L1_gnn_ln_g")),
        (k.ln_b[:, :], row("L1_gnn_ln_b")), (k.w_e2[:, :], i["L1_gnn_We2"]), (k.b_e2[:, :], row("L1_gnn_be2")),
        (k.w_g1[:, :], i["L1_gnn_Wg1"]), (k.b_g1[:, :], cols("L1_gnn_bg1")), (k.w_s1[:, :], i["L1_gnn_Ws1"]),
        (k.b_s1[:, :], cols("L1_gnn_bs1")),
        (k.w_g2[:, :, :], i["L1_gnn_Wg2"].rearrange("(q p) o -> p q o", p=P)), (k.b_g2[:, :], cols("L1_gnn_bg2")),
        (k.w_s2[:, :, :], i["L1_gnn_Ws2"].rearrange("(q p) o -> p q o", p=P)), (k.b_s2[:, :], cols("L1_gnn_bs2")),
        (k.w_d1[:, :, :], i["L1_gnn_Wd1"].rearrange("(q p) o -> p q o", p=P)), (k.b_d1[:, :], cols("L1_gnn_bd1")),
        (k.w_d2[:, :], i["L1_gnn_Wd2"]), (k.b_d2[:, :], row("L1_gnn_bd2")),
    ]
    k.late_loads = [(k.w_l2, i["L2_gnn_W"]), (k.w_l3a, i["L3_gnn_W1"]), (k.w_l3b, i["L3_gnn_W2"]),
                    (k.b_l2, row("L2_gnn_b")), (k.b_l3a, row("L3_gnn_b1")), (k.b_l3b, row("L3_gnn_b2"))]

    at = [SLOT]

    def take(n, dt=F32, rows=P):
        words = n if dt in (F32, I32) else -(-n // 2)
        view = arena[0:rows, at[0]:at[0] + words]
        at[0] += words
        return view if dt == F32 else view.bitcast(dt)

    def groups(view):
        return view.rearrange("p (g e) -> p g e", e=P)

    k.dst_rows, k.src_rows = groups(take(GROUPS * P, I32)), groups(take(GROUPS * P, I32))
    k.dst_rowsf, k.src_rowsf = groups(take(GROUPS * P)), groups(take(GROUPS * P))
    k.dst_cols, k.src_cols = take(GROUPS * P), take(GROUPS * P)
    k.node_number = take(PADDED, F16)
    k.zeros16, k.counts_row = take(P, BF16), take(PADDED, BF16)
    k.onehot_dst = take(STEP * P, BF16).rearrange("p (b e) -> p b e", b=STEP)
    wide = PART_END[1] - PART_START[1] + 1
    wide += -wide % 4
    k.onehot_src = take(STEP * wide, BF16).rearrange("p (b e) -> p b e", b=STEP)
    k.turn_rows = take(2 * PADDED, BF16).rearrange("p (b e) -> p b e", b=2)
    k.cand_lo = take(GROUPS * TILES).rearrange("p (t g) -> p t g", g=GROUPS)
    k.cand_hi = take(GROUPS * TILES).rearrange("p (t g) -> p t g", g=GROUPS)
    k.range_part = take(2 * TILES).rearrange("p (i t) -> p i t", i=2)
    k.chunk_number, k.chunk_next = take(GROUPS), take(GROUPS)
    k.chunk_max, k.chunk_min = take(GROUPS), take(GROUPS)
    k.tile_start, k.tile_end = take(TILES), take(TILES)
    k.lo, k.hi, k.take = take(1, rows=TILES), take(1, rows=TILES), take(1, rows=TILES)
    k.before = take(TILES + 1, rows=TILES)
    k.table, k.lo_row = take(2 * TILES + 1, I32, 1), take(TILES, rows=1)
    assert at[0] <= 6 * SLOT, at[0]


@contextmanager
def own_semaphores(nc, k):
    held = []

    def sem(name):
        held.append(nc.alloc_semaphore(name=name))
        return held[-1]

    k.sem = sem
    yield
    nc.clear_and_free_semaphores(held)
    nc.all_engine_barrier()


def graph_layers(nc, inputs, out):
    with ExitStack() as ctx:
        k = Kept()
        k.inputs, k.out = inputs, out
        k.x_dram, k.src, k.dst = inputs["x"], inputs["src"], inputs["dst"]
        place(nc, ctx, k)
        with own_semaphores(nc, k):
            load_inputs(nc, k)
            make_constants(nc, k)
            load_edges(nc, k)
            make_edge_tables(nc, k)
            build_counts(nc, k)
            turn_counts(nc, k)
            degrees(nc, k)
            gcn_batch_norm_layer(nc, k)
        with own_semaphores(nc, k):
            chan, gathered = first_attention(nc, k)
        with own_semaphores(nc, k):
            second_attention(nc, k, chan, gathered)
        with own_semaphores(nc, k):
            load_late_weights(nc, k)
            mean_layer(nc, k)
            gcn_layer(nc, k)
            store_output(nc, k)


_L1 = ("We1 be1 ln_g ln_b We2 be2 Wg1 as1 ad1 bg1 Ws1 bs1 Wg2 as2 ad2 bg2 Ws2 bs2 Wd1 bd1 Wd2 bd2").split()
_INS = (["x", "src", "dst"] + [f"L0_gnn_{n}" for n in ("W", "b", "gamma", "beta")]
        + [f"L1_gnn_{n}" for n in _L1] + ["L2_gnn_W", "L2_gnn_b"]
        + [f"L3_gnn_{n}" for n in ("W1", "b1", "W2", "b2")])


def kernel(**inputs):
    import numpy as _np
    import concourse.bacc as _bacc
    from concourse import mybir as _mybir
    from concourse.bass_utils import run_bass_kernel_spmd as _run

    nc = _bacc.Bacc("TRN2", target_bir_lowering=False, num_devices=1)
    arrays, aps = {}, {}
    for name in _INS:
        a = _np.ascontiguousarray(inputs[name])
        arrays[f"in_{name}_dram"] = a
        aps[name] = nc.dram_tensor(f"in_{name}_dram", a.shape, _mybir.dt.from_np(a.dtype), kind="ExternalInput").ap()
    out = nc.dram_tensor("out_0_dram", (3125, 128), _mybir.dt.float32, kind="ExternalOutput").ap()
    graph_layers(nc, aps, out)
    r = _run(nc, [arrays], core_ids=[0])
    return r.results[0]["out_0_dram"]
```
